# Optimizing a Trainium2 kernel written in Bass

```python
import numpy as np
import jax
import jax.numpy as jnp

def _softmax(x, axis=-1):
    return jax.nn.softmax(x, axis=axis)

def _gelu(x):
    return jax.nn.gelu(x, approximate=True)

def _silu(x):
    return jax.nn.silu(x)

def _sigmoid(x):
    return jax.nn.sigmoid(x)

def _layernorm(x, axis=-1, eps=1e-05):
    m = jnp.mean(x, axis=axis, keepdims=True)
    v = jnp.var(x, axis=axis, keepdims=True)
    return (x - m) / jnp.sqrt(v + eps)

def _scatter_add(tgt, idx, src, axis=0):
    return tgt.at[idx].add(src)

def _segment_sum(src, seg, n):
    return jax.ops.segment_sum(src, seg, n)
kernel_name = 'mk_rec_standalone_d1_rec_r8_585824'

def setup_inputs(seed: int=0):
    np.random.seed(seed)
    _w = jnp.asarray

    def _rec_inputs():
        import jax
        import jax.numpy as jnp
        _rk = jax.random.key(seed)
        r_x = -0.000154596 + 0.999967 * jax.random.normal(jax.random.fold_in(_rk, 1), (2048, 64, 128), jnp.float32)
        return r_x
    r_x = _rec_inputs()

    def _L0_rec_setup():
        import jax, jax.numpy as jnp
        import numpy as np
        B, F, E = (2048, 64, 128)
        ATT_D, HEADS = (32, 4)

        def _split_heads(t):
            b, f, _ = t.shape
            return t.reshape(b, f, HEADS, ATT_D).transpose(2, 0, 1, 3)
        key = jax.random.key(seed)
        k0, k1, k2, k3, k4 = jax.random.split(key, 5)
        return {'x': jax.random.normal(k0, (B, F, E), dtype=jnp.float32), 'W_query': jax.random.normal(k1, (E, ATT_D * HEADS), dtype=jnp.float32) * 0.05, 'W_key': jax.random.normal(k2, (E, ATT_D * HEADS), dtype=jnp.float32) * 0.05, 'W_value': jax.random.normal(k3, (E, ATT_D * HEADS), dtype=jnp.float32) * 0.05, 'W_res': jax.random.normal(k4, (E, ATT_D * HEADS), dtype=jnp.float32) * 0.05}
    _L0_rec_all = _L0_rec_setup()
    _L0_rec_in = {k: v for k, v in _L0_rec_all.items() if k in ('W_query', 'W_key', 'W_value', 'W_res')}
    del _L0_rec_all
    return {'r_x': r_x, 'L0_rec_W_query': _L0_rec_in['W_query'], 'L0_rec_W_key': _L0_rec_in['W_key'], 'L0_rec_W_value': _L0_rec_in['W_value'], 'L0_rec_W_res': _L0_rec_in['W_res']}

def reference(r_x, L0_rec_W_query, L0_rec_W_key, L0_rec_W_value, L0_rec_W_res):
    import jax
    import jax.numpy as jnp

    def _L0_rec_ref(x, W_query, W_key, W_value, W_res):
        import jax, jax.numpy as jnp
        import numpy as np
        B, F, E = (2048, 64, 128)
        ATT_D, HEADS = (32, 4)

        def _split_heads(t):
            b, f, _ = t.shape
            return t.reshape(b, f, HEADS, ATT_D).transpose(2, 0, 1, 3)
        q = _split_heads(jnp.einsum('bfe,ed->bfd', x, W_query))
        k = _split_heads(jnp.einsum('bfe,ed->bfd', x, W_key))
        v = _split_heads(jnp.einsum('bfe,ed->bfd', x, W_value))
        scores = jnp.einsum('hbqd,hbkd->hbqk', q, k)
        attn = jax.nn.softmax(scores, axis=-1)
        out = jnp.einsum('hbqk,hbkd->hbqd', attn, v)
        out = out.transpose(1, 2, 0, 3).reshape(x.shape[0], x.shape[1], HEADS * ATT_D)
        out = out + jnp.einsum('bfe,ed->bfd', x, W_res)
        return jax.nn.relu(out)
    y = _L0_rec_ref(r_x, L0_rec_W_query, L0_rec_W_key, L0_rec_W_value, L0_rec_W_res)
    return y

_drawn_inputs = setup_inputs


def setup_inputs(seed=0):
    import zlib

    import numpy as np

    out = dict(_drawn_inputs(seed))
    spreads = {}
    factors = {}
    for name, (base, spread) in spreads.items():
        noise = np.random.default_rng([zlib.crc32(name.encode()), seed]).standard_normal(out[name].shape)
        drawn = base * np.exp(spread * noise) if base else spread * noise
        out[name] = jnp.asarray(drawn.astype(out[name].dtype))
    for name, factor in factors.items():
        out[name] = (out[name] * factor).astype(out[name].dtype)
    return out
```

```python
from contextlib import ExitStack

import concourse.bass as bass
from concourse import mybir

F32 = mybir.dt.float32
F32R = mybir.dt.float32r
ALU = mybir.AluOpType
ACT = mybir.ActivationFunctionType
AX_X = mybir.AxisListType.X

P = 128
HEADS = 4
PAIRS = HEADS // 2
TILES = 2
SEQS = 2
BANK = 512


def attention_program(nc, x, w_query, w_key, w_value, w_res, out):
    B, F, E = x.shape
    D = w_query.shape[1] // HEADS
    COLS = HEADS * D
    assert E == P and COLS == P and F * SEQS == P and D * HEADS == P
    GROUPS = B // (SEQS * TILES)
    assert GROUPS * SEQS * TILES == B and GROUPS % 2 == 0 and GROUPS >= 8
    SCORES = HEADS * F
    VONE = 2 * D + 2
    BLOCKS = TILES * SEQS * PAIRS
    TOK = TILES * P

    x_groups = x.rearrange("(g t s) f e -> g (s f) t e", t=TILES, s=SEQS)
    out_groups = out.rearrange("(g t s) f e -> g (s f) t e", t=TILES, s=SEQS)

    with ExitStack() as ctx:
        def sb(name, shape, dt=F32):
            return ctx.enter_context(nc.sbuf_tensor(name, shape, dt))

        def bank(name):
            return ctx.enter_context(nc.psum_tensor(name, [P, BANK], F32))

        def sem(name):
            return ctx.enter_context(nc.semaphore(name))

        ident = sb("ident", [P, P])
        w_raw = sb("w_raw", [P, 4, COLS])
        w_hi = sb("w_hi", [P, 4, COLS], F32R)
        w_lo = sb("w_lo", [P, 4, COLS], F32R)
        x_in = sb("x_in", [P, 2, TILES, E])
        x_hi = [sb(f"x_hi{i}", [P, TOK], F32R) for i in range(2)]
        x_lo = [sb(f"x_lo{i}", [P, TOK], F32R) for i in range(2)]
        y = sb("y", [P, 2, TILES, COLS])
        q_t = sb("q_t", [P, TOK])
        k_diag = sb("k_diag", [P, TILES * SEQS, HEADS, F])
        v_diag = sb("v_diag", [P, BLOCKS, VONE])
        row_max = sb("row_max", [P, TILES * HEADS])
        shifted = sb("shifted", [P, TILES * SCORES])
        probs = sb("probs", [P, TILES * SCORES])
        probs_t = sb("probs_t", [P, TILES * PAIRS, P])
        inv_sum = sb("inv_sum", [P, TILES * HEADS])
        attn = sb("attn", [P, TILES * COLS])

        ps_x, ps_q, ps_k, ps_s, ps_pt, ps_o = [bank(f"ps_{n}") for n in ("x", "q", "k", "s", "pt", "o")]
        ps_vr = [bank(f"ps_vr{i}") for i in range(2)]

        w_loaded = sem("w_loaded")
        x_loaded = [sem(f"x_loaded{i}") for i in range(2)]
        y_stored = [sem(f"y_stored{i}") for i in range(2)]
        ident_zero, ident_ready = sem("ident_zero"), sem("ident_ready")
        diag_zero, ones_ready = sem("diag_zero"), sem("ones_ready")
        whi_ready, wlo_ready = sem("whi_ready"), sem("wlo_ready")
        xt_done, q_done, k_done, vr_done = sem("xt_done"), sem("q_done"), sem("k_done"), sem("vr_done")
        s_done, pt_done, o_done = sem("s_done"), sem("pt_done"), sem("o_done")
        xhi_ready, xlo_ready = sem("xhi_ready"), sem("xlo_ready")
        q_ready, k_ready = sem("q_ready"), sem("k_ready")
        v_ready = sem("v_ready")
        max_ready, shifted_ready, probs_ready = sem("max_ready"), sem("shifted_ready"), sem("probs_ready")
        pt_ready, inv_ready, attn_ready = sem("pt_ready"), sem("inv_ready"), sem("attn_ready")
        sum_ready, y_ready = sem("sum_ready"), sem("y_ready")

        block = ctx.enter_context(nc.Block())

        def run(engine, step, first):
            for g in range(first, 4):
                step(g, g % 2)
            with engine.Fori(2, GROUPS // 2 - 1) as i:
                for parity in range(2):
                    step(i * 2 + parity, parity)
            for g in range(GROUPS - 2, GROUPS + 2):
                step(g, g % 2)

        def has(g, least=0):
            return not isinstance(g, int) or least <= g < GROUPS

        def dma_count(g, parity):
            return (g - parity) * 8 + 16

        def heads_of(ap):
            return ap.rearrange("p (t w q j d) -> p t w q j d", t=TILES, w=2, q=PAIRS, j=2)

        @block.sync
        def _(sp):
            def load(g, parity):
                sp.dma_start(x_in[:, parity], x_groups[g]).then_inc(x_loaded[parity], 16)

            load(0, 0)
            load(1, 1)

            def step(g, parity):
                if has(g + 2):
                    if has(g, 0):
                        sp.wait_ge(xt_done, g + 1)
                    load(g + 2, parity)
                if has(g - 2):
                    sp.wait_ge(y_ready, g - 1)
                    sp.dma_start(out_groups[g - 2], y[:, parity]).then_inc(y_stored[parity], 16)

            run(sp, step, 0)
            for parity in range(2):
                sp.wait_ge(y_stored[parity], 8 * GROUPS)

        @block.gpsimd
        def _(pool):
            nc.gpsimd.memset(ident[:, :], 0.0).then_inc(ident_zero, 1)
            pool.wait_ge(ident_zero, 1)
            nc.gpsimd.affine_select(out=ident[:, :], in_=ident[:, :], compare_op=ALU.not_equal, fill=1.0, base=0,
                                    pattern=[[-1, P]], channel_multiplier=1).then_inc(ident_ready, 1)

        @block.tensor
        def _(pe):
            def transpose_x(g, parity):
                pe.wait_ge(x_loaded[parity], dma_count(g, parity))
                for t in range(TILES):
                    last = nc.tensor.transpose(ps_x[:, t * P:(t + 1) * P], x_in[:, parity, t, :], ident[:, :])
                last.then_inc(xt_done, 1)

            def project_qk(g, parity):
                pe.wait_ge(xlo_ready, g + 1)
                for w, ps, done in ((0, ps_q, q_done), (1, ps_k, k_done)):
                    nc.tensor.matmul(ps[:, 0:TOK], w_hi[:, w, :], x_hi[parity][:, :], start=True, stop=False)
                    nc.tensor.matmul(ps[:, 0:TOK], w_lo[:, w, :], x_hi[parity][:, :], start=False, stop=False)
                    nc.tensor.matmul(ps[:, 0:TOK], w_hi[:, w, :], x_lo[parity][:, :], start=False,
                                     stop=True).then_inc(done, 1)

            def step(g, parity):
                if has(g):
                    pe.wait_ge(q_ready, g + 1)
                    pe.wait_ge(k_ready, g + 1)
                    if has(g, 1):
                        pe.wait_ge(shifted_ready, g)
                    for t in range(TILES):
                        for s in range(SEQS):
                            last = nc.tensor.matmul(
                                ps_s[s * F:(s + 1) * F, t * SCORES:(t + 1) * SCORES],
                                q_t[:, t * P + s * F:t * P + (s + 1) * F],
                                k_diag[:, t * SEQS + s, :, :].rearrange("p h f -> p (h f)"), start=True, stop=True)
                    last.then_inc(s_done, 1)
                if has(g - 1):
                    pe.wait_ge(probs_ready, g)
                    if has(g - 1, 1):
                        pe.wait_ge(pt_ready, g - 1)
                    for c in range(TILES * PAIRS):
                        last = nc.tensor.transpose(ps_pt[:, c * P:(c + 1) * P], probs[:, c * P:(c + 1) * P],
                                                   ident[:, :])
                    last.then_inc(pt_done, 1)
                if has(g + 1):
                    project_qk(g + 1, 1 - parity)
                if has(g + 2):
                    transpose_x(g + 2, parity)
                if has(g - 1):
                    pe.wait_ge(pt_ready, g)
                    pe.wait_ge(v_ready, g)
                    if has(g - 1, 1):
                        pe.wait_ge(attn_ready, g - 1)
                    for t in range(TILES):
                        for q in range(PAIRS):
                            for s in range(SEQS):
                                c = t * PAIRS + q
                                last = nc.tensor.matmul(
                                    ps_o[s * F:(s + 1) * F, c * VONE:(c + 1) * VONE],
                                    probs_t[:, c, s * F:(s + 1) * F],
                                    v_diag[:, (t * SEQS + s) * PAIRS + q, :], start=True, stop=True)
                    last.then_inc(o_done, 1)
                if has(g):
                    if has(g, 2):
                        pe.wait_ge(sum_ready, g - 1)
                    vr, hi, lo = ps_vr[parity], x_hi[parity], x_lo[parity]
                    w_vr_hi = w_hi[:, 2:4, :].rearrange("p w c -> p (w c)")
                    w_vr_lo = w_lo[:, 2:4, :].rearrange("p w c -> p (w c)")
                    for t in range(TILES):
                        cols, tok = slice(t * 2 * COLS, (t + 1) * 2 * COLS), slice(t * P, (t + 1) * P)
                        nc.tensor.matmul(vr[:, cols], hi[:, tok], w_vr_hi, start=True, stop=False)
                        nc.tensor.matmul(vr[:, cols], hi[:, tok], w_vr_lo, start=False, stop=False)
                        last = nc.tensor.matmul(vr[:, cols], lo[:, tok], w_vr_hi, start=False, stop=True)
                    last.then_inc(vr_done, 1)

            pe.wait_ge(ident_ready, 1)
            transpose_x(0, 0)
            pe.wait_ge(wlo_ready, 1)
            project_qk(0, 0)
            transpose_x(1, 1)
            pe.wait_ge(diag_zero, 1)
            pe.wait_ge(ones_ready, 1)
            run(pe, step, 0)

        @block.scalar
        def _(act):
            def copy_k(g):
                act.wait_ge(k_done, g + 1)
                for h in range(HEADS):
                    rows = slice(h * D, (h + 1) * D)
                    last = nc.scalar.copy(k_diag[rows, :, h, :],
                                          ps_k[rows, 0:TOK].rearrange("p (b f) -> p b f", f=F))
                last.then_inc(k_ready, 1)

            def copy_v(g, parity):
                blocks = v_diag[:, :, :].rearrange("p (t s q) c -> p t s q c", t=TILES, s=SEQS)
                act.wait_ge(vr_done, g + 1)
                for s in range(SEQS):
                    for j in range(2):
                        last = nc.scalar.copy(blocks[j * F:(j + 1) * F, :, s, :, j * D:(j + 1) * D],
                                              heads_of(ps_vr[parity][:, :])[s * F:(s + 1) * F, :, 0, :, j, :])
                last.then_inc(v_ready, 1)

            def copy_xhi(g, parity):
                act.wait_ge(xt_done, g + 1)
                if has(g - 2):
                    act.wait_ge(vr_done, g - 1)
                nc.scalar.copy(x_hi[parity][:, :], ps_x[:, 0:TOK]).then_inc(xhi_ready, 1)

            def step(g, parity):
                if has(g - 1):
                    act.wait_ge(pt_done, g)
                    nc.scalar.copy(probs_t[:, :, :].rearrange("p c q -> p (c q)"), ps_pt[:, :]).then_inc(pt_ready, 1)
                if has(g + 1):
                    copy_k(g + 1)
                if has(g):
                    act.wait_ge(shifted_ready, g + 1)
                    nc.scalar.activation(probs[:, :], shifted[:, :], ACT.Exp).then_inc(probs_ready, 1)
                if has(g + 2):
                    copy_xhi(g + 2, parity)
                if has(g):
                    copy_v(g, parity)

            for n, w in enumerate((w_query, w_key, w_value, w_res)):
                act.dma_start(w_raw[:, n, :], w).then_inc(w_loaded, 16)
            act.wait_ge(w_loaded, 64)
            nc.scalar.copy(w_hi[:, :, :], w_raw[:, :, :]).then_inc(whi_ready, 1)
            copy_xhi(0, 0)
            act.wait_ge(diag_zero, 1)
            copy_k(0)
            copy_xhi(1, 1)
            run(act, step, 0)

        @block.vector
        def _(dve):
            def split_xlo(g, parity):
                dve.wait_ge(xhi_ready, g + 1)
                nc.vector.tensor_tensor(x_lo[parity][:, :], ps_x[:, 0:TOK], x_hi[parity][:, :].bitcast(F32),
                                        ALU.subtract).then_inc(xlo_ready, 1)

            def copy_q(g):
                dve.wait_ge(q_done, g + 1)
                nc.vector.tensor_copy(q_t[:, :], ps_q[:, 0:TOK]).then_inc(q_ready, 1)

            def step(g, parity):
                scores = ps_s[:, :].rearrange("p (h f) -> p h f", f=F)
                if has(g):
                    dve.wait_ge(s_done, g + 1)
                    nc.vector.reduce_max(row_max[:, :], scores, AX_X).then_inc(max_ready, 1)
                if has(g - 2):
                    dve.wait_ge(sum_ready, g - 1)
                    nc.vector.tensor_scalar(y[:, parity], y[:, parity], 0.0, None, ALU.max).then_inc(y_ready, 1)
                if has(g):
                    dve.wait_ge(max_ready, g + 1)
                    if has(g, 1):
                        dve.wait_ge(probs_ready, g)
                    nc.vector.tensor_tensor(shifted[:, :].rearrange("p (h f) -> p h f", f=F), scores,
                                            row_max[:, :].unsqueeze(2).to_broadcast([P, TILES * HEADS, F]),
                                            ALU.subtract).then_inc(shifted_ready, 1)
                if has(g + 1):
                    copy_q(g + 1)
                if has(g - 1):
                    sums = ps_o[:, 0:TILES * PAIRS * VONE].rearrange("p (c w) -> p c w", w=VONE)
                    dve.wait_ge(o_done, g)
                    nc.vector.reciprocal(inv_sum[:, :].rearrange("p (c j) -> p c j", j=2),
                                         sums[:, :, 2 * D:]).then_inc(inv_ready, 1)
                    dve.wait_ge(inv_ready, g)
                    nc.vector.tensor_tensor(
                        attn[:, :].rearrange("p (c j d) -> p c j d", j=2, d=D),
                        sums[:, :, 0:2 * D].rearrange("p c (j d) -> p c j d", j=2),
                        inv_sum[:, :].rearrange("p (c j) -> p c j", j=2).unsqueeze(3)
                        .to_broadcast([P, TILES * PAIRS, 2, D]),
                        ALU.mult).then_inc(attn_ready, 1)
                    dve.wait_ge(attn_ready, g)
                    if has(g - 1, 2):
                        dve.wait_ge(y_stored[1 - parity], dma_count(g - 3, 1 - parity))
                    res = ps_vr[1 - parity][:, :].rearrange("p (t w c) -> p t w c", t=TILES, w=2)[:, :, 1, :]
                    nc.vector.tensor_tensor(y[:, 1 - parity], res,
                                            attn[:, :].rearrange("p (t c) -> p t c", t=TILES),
                                            ALU.add).then_inc(sum_ready, 1)
                if has(g + 2):
                    split_xlo(g + 2, parity)

            nc.vector.memset(k_diag[:, :, :, :], 0.0)
            nc.vector.memset(v_diag[:, :, :], 0.0).then_inc(diag_zero, 1)
            dve.wait_ge(diag_zero, 1)
            nc.vector.memset(v_diag[0:F, :, 2 * D:2 * D + 1], 1.0)
            nc.vector.memset(v_diag[F:P, :, 2 * D + 1:VONE], 1.0).then_inc(ones_ready, 1)
            dve.wait_ge(whi_ready, 1)
            nc.vector.tensor_tensor(w_lo[:, :, :], w_raw[:, :, :], w_hi[:, :, :].bitcast(F32),
                                    ALU.subtract).then_inc(wlo_ready, 1)
            split_xlo(0, 0)
            copy_q(0)
            split_xlo(1, 1)
            run(dve, step, 0)


_INS = ["r_x", "L0_rec_W_query", "L0_rec_W_key", "L0_rec_W_value", "L0_rec_W_res"]


def kernel(**inputs):
    import numpy as _np
    import concourse.bacc as _bacc
    from concourse import mybir as _mybir
    from concourse.bass_utils import run_bass_kernel_spmd as _run

    nc = _bacc.Bacc("TRN2", target_bir_lowering=False, num_devices=1)
    arrays, args = {}, []
    for name in _INS:
        a = _np.ascontiguousarray(inputs[name])
        arrays[f"in_{name}_dram"] = a
        args.append(nc.dram_tensor(f"in_{name}_dram", a.shape, _mybir.dt.from_np(a.dtype), kind="ExternalInput").ap())
    shape = inputs["r_x"].shape
    out = nc.dram_tensor("out_0_dram", shape, _mybir.dt.float32, kind="ExternalOutput").ap()
    attention_program(nc, *args, out)
    r = _run(nc, [arrays], core_ids=[0])
    return r.results[0]["out_0_dram"]
```
